# Optimizing a Trainium2 kernel written in Bass

```python
import numpy as np
import jax
import jax.numpy as jnp

def _softmax(x, axis=-1):
    return jax.nn.softmax(x, axis=axis)
def _gelu(x):
    return jax.nn.gelu(x, approximate=True)
def _silu(x):
    return jax.nn.silu(x)
def _sigmoid(x):
    return jax.nn.sigmoid(x)
def _layernorm(x, axis=-1, eps=1e-5):
    m = jnp.mean(x, axis=axis, keepdims=True)
    v = jnp.var(x, axis=axis, keepdims=True)
    return (x - m) / jnp.sqrt(v + eps)
def _scatter_add(tgt, idx, src, axis=0):
    return tgt.at[idx].add(src)
def _segment_sum(src, seg, n):
    return jax.ops.segment_sum(src, seg, n)

kernel_name = 'mk_rec_standalone_d1_rec_a5d531'

def setup_inputs(seed: int = 0):
    np.random.seed(seed)
    _w = jnp.asarray
    def _rec_inputs():
        import jax
        import jax.numpy as jnp
        _rk = jax.random.key(seed)
        r_sparse_features = -7.97023e-05 + 0.9999 * jax.random.normal(jax.random.fold_in(_rk, 1), (16384, 3328), jnp.float32)
        r_dense_features = -0.000514642 + 1.00011 * jax.random.normal(jax.random.fold_in(_rk, 2), (16384, 128), jnp.float32)
        return r_sparse_features, r_dense_features
    r_sparse_features, r_dense_features = _rec_inputs()
    def _L0_rec_setup():
        import jax, jax.numpy as jnp
        import numpy as np
        NUM_FEATURES = 26
        EMB_DIM = 128
        BATCH = 16384
        DENSE_DIM = 128
        _IU, _JU = np.triu_indices(NUM_FEATURES, k=1)
        key = jax.random.key(seed)
        k1, k2 = jax.random.split(key)
        sparse_features = jax.random.normal(k1, (BATCH, NUM_FEATURES * EMB_DIM), dtype=jnp.float32)
        dense_features = jax.random.normal(k2, (BATCH, DENSE_DIM), dtype=jnp.float32)
        return {'sparse_features': sparse_features, 'dense_features': dense_features}
    _L0_rec_all = _L0_rec_setup()
    _L0_rec_in = {k: v for k, v in _L0_rec_all.items() if k in ()}
    del _L0_rec_all

    return {
        "r_sparse_features": r_sparse_features,
        "r_dense_features": r_dense_features,
    }

def reference(r_sparse_features, r_dense_features):
    import jax
    import jax.numpy as jnp
    def _L0_rec_ref(sparse_features, dense_features):
        import jax, jax.numpy as jnp
        import numpy as np
        NUM_FEATURES = 26
        EMB_DIM = 128
        BATCH = 16384
        DENSE_DIM = 128
        _IU, _JU = np.triu_indices(NUM_FEATURES, k=1)
        B = sparse_features.shape[0]
        emb = sparse_features.reshape(B, NUM_FEATURES, EMB_DIM)
        gram = jnp.einsum('bfd,bgd->bfg', emb, emb)
        interactions = gram[:, _IU, _JU]
        return jnp.concatenate([sparse_features, interactions, dense_features], axis=1)

    y = _L0_rec_ref(r_sparse_features, r_dense_features)
    return y


_drawn_inputs = setup_inputs


def setup_inputs(seed=0):
    import zlib

    import numpy as np

    out = dict(_drawn_inputs(seed))
    spreads = {}
    factors = {}
    for name, (base, spread) in spreads.items():
        noise = np.random.default_rng([zlib.crc32(name.encode()), seed]).standard_normal(out[name].shape)
        drawn = base * np.exp(spread * noise) if base else spread * noise
        out[name] = jnp.asarray(drawn.astype(out[name].dtype))
    for name, factor in factors.items():
        out[name] = (out[name] * factor).astype(out[name].dtype)
    return out
```

```python
from contextlib import ExitStack

import concourse.bass as bass
from concourse import mybir

F32 = mybir.dt.float32
ALU = mybir.AluOpType

P = 128
QUAD = 32
NQUAD = P // QUAD
SLOTS = 8
AHEAD = 6
TCHUNK = 8
GCHUNK = 8
BANK = 512


def interactions_kernel(nc, sparse, dense, out):
    batch, sparse_w = sparse.shape
    dense_w = dense.shape[1]
    D = P
    NF = sparse_w // D
    NL = NF - 1
    pairs = NF * NL // 2
    row_w = sparse_w + pairs
    tiles = batch // P
    groups = tiles // SLOTS
    assert out.shape[1] == row_w + dense_w and tiles % SLOTS == 0 and NF <= QUAD

    first_pair = [f * NL - f * (f - 1) // 2 for f in range(NL)]
    tchunks = [(f, min(TCHUNK, NF - f)) for f in range(0, NF, TCHUNK)]
    gchunks = QUAD // GCHUNK
    PER_BANK = GCHUNK // 2
    TC, GC = len(tchunks), gchunks
    assert TC % 2 == 0 and GC % 2 == 0

    sparse_t = sparse.rearrange("(t p) n -> t p n", p=P)
    out_t = out.rearrange("(t p) n -> t p n", p=P)
    dense_g = dense.rearrange("(g b) n -> g b n", g=groups)
    out_g = out.rearrange("(g b) n -> g b n", g=groups)

    with ExitStack() as ctx:
        def sb(name, shape):
            return ctx.enter_context(nc.sbuf_tensor(name, shape, F32))

        def ps(name):
            return ctx.enter_context(nc.psum_tensor(name, [P, 2, BANK], F32))

        def sem(name):
            return ctx.enter_context(nc.semaphore(name))

        row_buf = sb("row_buf", [P, SLOTS, row_w])
        emb_t = [sb(f"emb_t{i}", [P, QUAD, NQUAD, QUAD]) for i in range(2)]
        gram = [sb(f"gram{i}", [P, NL, QUAD]) for i in range(2)]
        gram_rows = [sb(f"gram_rows{i}", [P, NL, QUAD]) for i in range(2)]
        ident = sb("ident", [P, P])
        turned_ps = [ps(f"turned_ps{i}") for i in range(2)]
        gram_ps = [ps(f"gram_ps{i}") for i in range(2)]

        loaded = [sem(f"loaded{k}") for k in range(SLOTS)]
        stored = [sem(f"stored{k}") for k in range(SLOTS)]
        packed = [sem(f"packed{i}") for i in range(2)]
        pack_begun = sem("pack_begun")
        dense_copied = sem("dense_copied")
        zeroed = sem("zeroed")
        ident_ready = sem("ident_ready")
        turned = sem("turned")
        gathered = [sem(f"gathered{i}") for i in range(2)]
        gram_done = [sem(f"gram_done{i}") for i in range(2)]
        gram_moved = [sem(f"gram_moved{i}") for i in range(2)]
        gram_read = [sem(f"gram_read{i}") for i in range(2)]

        block = ctx.enter_context(nc.Block())

        START = 1

        def earlier(g, u):
            return g * (SLOTS // 2) + u // 2

        @block.sync
        def _(sp):
            def load(g, u, first=False):
                g, u = g + u // SLOTS, u % SLOTS
                if not first:
                    sp.wait_ge(stored[u], 16 * g)
                sp.dma_start(row_buf[:, u, 0:sparse_w], sparse_t[g * SLOTS + u]).then_inc(loaded[u], 16)

            def group(g, first=False, last=False):
                for u in range(SLOTS):
                    sp.wait_ge(packed[u % 2], START + earlier(g, u) + 1)
                    sp.dma_start(out_t[g * SLOTS + u][:, 0:row_w], row_buf[:, u, :]).then_inc(stored[u], 16)
                    if not (first and u + AHEAD < SLOTS or last and u + AHEAD >= SLOTS):
                        load(g, u + AHEAD)
                sp.dma_start(out_g[g][:, row_w:], dense_g[g]).then_inc(dense_copied, 16)

            for u in range(SLOTS):
                load(0, u, first=True)
            group(0, first=True)
            with sp.Fori(1, groups - 1) as g:
                group(g)
            group(groups - 1, last=True)
            for u in range(SLOTS):
                sp.wait_ge(stored[u], 16 * groups)
            sp.wait_ge(dense_copied, 16 * groups)

        @block.tensor
        def _(pe):
            def turn(g, u, c):
                g, u = g + u // SLOTS, u % SLOTS
                f0, nf = tchunks[c]
                if c == 0:
                    pe.wait_ge(loaded[u], 16 * (g + 1))
                pe.wait_ge(gathered[c % 2], START + (g * SLOTS + u) * (TC // 2) + c // 2)
                for j in range(nf):
                    f = f0 + j
                    at = turned_ps[c % 2][:, j // 4, (j % 4) * P:(j % 4 + 1) * P]
                    last = nc.tensor.transpose(at, row_buf[:, u, f * D:(f + 1) * D], ident[:, :])
                last.then_inc(turned, 1)

            def products(g, u, c):
                emb = emb_t[u % 2]
                if c == 0:
                    for b in range(2):
                        pe.wait_ge(gathered[b], START + (g * SLOTS + (u + 1)) * (TC // 2))
                pe.wait_ge(gram_moved[c % 2], START + (g * SLOTS + u) * (GC // 2) + c // 2)
                for j in range(GCHUNK):
                    q = c * GCHUNK + j
                    n = NQUAD * NL
                    at = gram_ps[c % 2][:, j // PER_BANK, (j % PER_BANK) * n:(j % PER_BANK + 1) * n]
                    last = nc.tensor.matmul(at, emb[:, q, :, :].rearrange("d i f -> d (i f)"), emb[:, q, :, 0:NL], start=True, stop=True)
                last.then_inc(gram_done[u % 2], 1)

            def group(g, last):
                for u in range(SLOTS):
                    for c in range(max(TC, GC)):
                        if c < TC and not (last and u == SLOTS - 1):
                            turn(g, u + 1, c)
                        if c < GC:
                            products(g, u, c)

            for i in range(2):
                pe.sem_inc(gram_done[i], START)
            pe.wait_ge(ident_ready, 1)
            for c in range(TC):
                turn(0, 0, c)
            with pe.Fori(0, groups - 1) as g:
                group(g, False)
            group(groups - 1, True)

        @block.vector
        def _(dve):
            def gather(g, u, c):
                f0, nf = tchunks[c]
                dst = emb_t[u % 2][:, :, :, f0:f0 + nf].rearrange("d q i f -> d i q f")
                src = turned_ps[c % 2][:, :, :].rearrange("d a (b i q) -> d i q (a b)", b=4, i=NQUAD)[:, :, :, 0:nf]
                if c == 0:
                    dve.wait_ge(gram_done[u % 2], START + earlier(g, u) * GC)
                dve.wait_ge(turned, (g * SLOTS + u) * TC + (c + 1))
                nc.vector.tensor_copy(dst, src).then_inc(gathered[c % 2], 1)

            def turn_blocks(g, u):
                for b in range(2):
                    dve.wait_ge(gram_moved[b], START + (g * SLOTS + (u + 1)) * (GC // 2))
                dve.wait_ge(packed[u % 2], START + earlier(g, u))
                nc.vector.transpose(gram_rows[u % 2][:, :, :], gram[u % 2][:, :, :]).then_inc(gram_read[u % 2], 1)

            def group(g, last):
                for u in range(SLOTS):
                    if not (last and u == SLOTS - 1):
                        for c in range(TC):
                            gather(g + (u + 1) // SLOTS, (u + 1) % SLOTS, c)
                    turn_blocks(g, u)

            for i in range(2):
                dve.sem_inc(gathered[i], START)
                dve.sem_inc(gram_read[i], START)
                nc.vector.memset(emb_t[i][:, :, :, NF:], 0.0).then_inc(zeroed, 1)
            dve.wait_ge(zeroed, 2)
            for c in range(TC):
                gather(0, 0, c)
            with dve.Fori(0, groups - 1) as g:
                group(g, False)
            group(groups - 1, True)

        @block.scalar
        def _(act):
            for i in range(2):
                act.sem_inc(gram_moved[i], START)
            with act.Fori(0, groups) as g:
                for u in range(SLOTS):
                    for c in range(GC):
                        act.wait_ge(gram_done[u % 2], START + earlier(g, u) * GC + (c + 1))
                        if c == 0:
                            act.wait_ge(gram_read[u % 2], START + earlier(g, u))
                        for i in range(NQUAD):
                            part = slice(i * QUAD, (i + 1) * QUAD)
                            src = gram_ps[c % 2][part, :, 0:PER_BANK * NQUAD * NL].rearrange(
                                "g b (q i f) -> g b q i f", q=PER_BANK, i=NQUAD)[:, :, :, i, :]
                            dst = gram[u % 2][part, :, c * GCHUNK:(c + 1) * GCHUNK].rearrange(
                                "g f (b q) -> g b q f", b=2)
                            last = nc.scalar.copy(dst, src)
                        last.then_inc(gram_moved[c % 2], 1)

        @block.gpsimd
        def _(pool):
            for i in range(2):
                pool.sem_inc(packed[i], START)
            nc.gpsimd.memset(ident[:], 0.0).then_inc(zeroed, 1)
            pool.wait_ge(zeroed, 3)
            nc.gpsimd.affine_select(out=ident[:], in_=ident[:], compare_op=ALU.not_equal, fill=1.0,
                                    base=0, pattern=[[-1, P]], channel_multiplier=1).then_inc(ident_ready, 1)
            with pool.Fori(0, groups) as g:
                for u in range(SLOTS):
                    pool.wait_ge(gram_read[u % 2], START + earlier(g, u) + 1)
                    pool.sem_inc(pack_begun, 1)
                    for f in range(NL):
                        at = sparse_w + first_pair[f]
                        last = nc.gpsimd.tensor_copy(row_buf[:, u, at:at + NL - f],
                                                     gram_rows[u % 2][:, f, f + 1:NF])
                    last.then_inc(packed[u % 2], 1)


_OUT = (16384, 3781)


def kernel(r_sparse_features, r_dense_features):
    import numpy as np
    import concourse.bacc as bacc
    from concourse.bass_utils import run_bass_kernel_spmd

    nc = bacc.Bacc("TRN2", target_bir_lowering=False, num_devices=1)
    arrays = {"sparse_dram": np.ascontiguousarray(r_sparse_features),
              "dense_dram": np.ascontiguousarray(r_dense_features)}
    args = [nc.dram_tensor(n, a.shape, F32, kind="ExternalInput").ap() for n, a in arrays.items()]
    out = nc.dram_tensor("out_dram", _OUT, F32, kind="ExternalOutput").ap()
    interactions_kernel(nc, *args, out)
    r = run_bass_kernel_spmd(nc, [arrays], core_ids=[0])
    return r.results[0]["out_dram"]
```
